# Optimizing a Trainium2 kernel written in Bass

```python
import numpy as np
import jax
import jax.numpy as jnp

def _softmax(x, axis=-1):
    return jax.nn.softmax(x, axis=axis)

def _gelu(x):
    return jax.nn.gelu(x, approximate=True)

def _silu(x):
    return jax.nn.silu(x)

def _sigmoid(x):
    return jax.nn.sigmoid(x)

def _layernorm(x, axis=-1, eps=1e-05):
    m = jnp.mean(x, axis=axis, keepdims=True)
    v = jnp.var(x, axis=axis, keepdims=True)
    return (x - m) / jnp.sqrt(v + eps)

def _scatter_add(tgt, idx, src, axis=0):
    return tgt.at[idx].add(src)

def _segment_sum(src, seg, n):
    return jax.ops.segment_sum(src, seg, n)
kernel_name = 'mk_dlrm_tower_d1_rec_r8_0105bd'

def setup_inputs(seed: int=0):
    np.random.seed(seed)
    _w = jnp.asarray

    def _rec_inputs():
        import jax
        import jax.numpy as jnp
        _tk = jax.random.key(seed)
        dense_ctx = jax.random.normal(jax.random.fold_in(_tk, 190), (2048, 16), jnp.float32)
        ids = jnp.stack([jax.random.randint(jax.random.fold_in(_tk, 200 + f), (2048,), 0, v, jnp.int32) for f, v in enumerate([1000, 1250, 1000, 12500, 1000, 125000, 12500, 1000, 1000, 12500, 12500, 1000, 125000, 1000, 125000, 1250, 125000, 1250, 1000, 1250, 1000, 125000, 125000, 1000, 12500, 125000, 1000, 12500, 1250, 12500, 1250, 1000, 1000, 1000, 1000, 1250, 1000, 1250, 1000, 1250])], axis=1)
        tbl_0 = 0.05 * jax.random.normal(jax.random.fold_in(_tk, 500 + 0), (1000, 32), jnp.float32)
        tbl_1 = 0.05 * jax.random.normal(jax.random.fold_in(_tk, 500 + 1), (1250, 32), jnp.float32)
        tbl_2 = 0.05 * jax.random.normal(jax.random.fold_in(_tk, 500 + 2), (1000, 32), jnp.float32)
        tbl_3 = 0.05 * jax.random.normal(jax.random.fold_in(_tk, 500 + 3), (12500, 32), jnp.float32)
        tbl_4 = 0.05 * jax.random.normal(jax.random.fold_in(_tk, 500 + 4), (1000, 32), jnp.float32)
        tbl_5 = 0.05 * jax.random.normal(jax.random.fold_in(_tk, 500 + 5), (125000, 32), jnp.float32)
        tbl_6 = 0.05 * jax.random.normal(jax.random.fold_in(_tk, 500 + 6), (12500, 32), jnp.float32)
        tbl_7 = 0.05 * jax.random.normal(jax.random.fold_in(_tk, 500 + 7), (1000, 32), jnp.float32)
        tbl_8 = 0.05 * jax.random.normal(jax.random.fold_in(_tk, 500 + 8), (1000, 32), jnp.float32)
        tbl_9 = 0.05 * jax.random.normal(jax.random.fold_in(_tk, 500 + 9), (12500, 32), jnp.float32)
        tbl_10 = 0.05 * jax.random.normal(jax.random.fold_in(_tk, 500 + 10), (12500, 32), jnp.float32)
        tbl_11 = 0.05 * jax.random.normal(jax.random.fold_in(_tk, 500 + 11), (1000, 32), jnp.float32)
        tbl_12 = 0.05 * jax.random.normal(jax.random.fold_in(_tk, 500 + 12), (125000, 32), jnp.float32)
        tbl_13 = 0.05 * jax.random.normal(jax.random.fold_in(_tk, 500 + 13), (1000, 32), jnp.float32)
        tbl_14 = 0.05 * jax.random.normal(jax.random.fold_in(_tk, 500 + 14), (125000, 32), jnp.float32)
        tbl_15 = 0.05 * jax.random.normal(jax.random.fold_in(_tk, 500 + 15), (1250, 32), jnp.float32)
        tbl_16 = 0.05 * jax.random.normal(jax.random.fold_in(_tk, 500 + 16), (125000, 32), jnp.float32)
        tbl_17 = 0.05 * jax.random.normal(jax.random.fold_in(_tk, 500 + 17), (1250, 32), jnp.float32)
        tbl_18 = 0.05 * jax.random.normal(jax.random.fold_in(_tk, 500 + 18), (1000, 32), jnp.float32)
        tbl_19 = 0.05 * jax.random.normal(jax.random.fold_in(_tk, 500 + 19), (1250, 32), jnp.float32)
        tbl_20 = 0.05 * jax.random.normal(jax.random.fold_in(_tk, 500 + 20), (1000, 32), jnp.float32)
        tbl_21 = 0.05 * jax.random.normal(jax.random.fold_in(_tk, 500 + 21), (125000, 32), jnp.float32)
        tbl_22 = 0.05 * jax.random.normal(jax.random.fold_in(_tk, 500 + 22), (125000, 32), jnp.float32)
        tbl_23 = 0.05 * jax.random.normal(jax.random.fold_in(_tk, 500 + 23), (1000, 32), jnp.float32)
        tbl_24 = 0.05 * jax.random.normal(jax.random.fold_in(_tk, 500 + 24), (12500, 32), jnp.float32)
        tbl_25 = 0.05 * jax.random.normal(jax.random.fold_in(_tk, 500 + 25), (125000, 32), jnp.float32)
        tbl_26 = 0.05 * jax.random.normal(jax.random.fold_in(_tk, 500 + 26), (1000, 32), jnp.float32)
        tbl_27 = 0.05 * jax.random.normal(jax.random.fold_in(_tk, 500 + 27), (12500, 32), jnp.float32)
        tbl_28 = 0.05 * jax.random.normal(jax.random.fold_in(_tk, 500 + 28), (1250, 32), jnp.float32)
        tbl_29 = 0.05 * jax.random.normal(jax.random.fold_in(_tk, 500 + 29), (12500, 32), jnp.float32)
        tbl_30 = 0.05 * jax.random.normal(jax.random.fold_in(_tk, 500 + 30), (1250, 32), jnp.float32)
        tbl_31 = 0.05 * jax.random.normal(jax.random.fold_in(_tk, 500 + 31), (1000, 32), jnp.float32)
        tbl_32 = 0.05 * jax.random.normal(jax.random.fold_in(_tk, 500 + 32), (1000, 32), jnp.float32)
        tbl_33 = 0.05 * jax.random.normal(jax.random.fold_in(_tk, 500 + 33), (1000, 32), jnp.float32)
        tbl_34 = 0.05 * jax.random.normal(jax.random.fold_in(_tk, 500 + 34), (1000, 32), jnp.float32)
        tbl_35 = 0.05 * jax.random.normal(jax.random.fold_in(_tk, 500 + 35), (1250, 32), jnp.float32)
        tbl_36 = 0.05 * jax.random.normal(jax.random.fold_in(_tk, 500 + 36), (1000, 32), jnp.float32)
        tbl_37 = 0.05 * jax.random.normal(jax.random.fold_in(_tk, 500 + 37), (1250, 32), jnp.float32)
        tbl_38 = 0.05 * jax.random.normal(jax.random.fold_in(_tk, 500 + 38), (1000, 32), jnp.float32)
        tbl_39 = 0.05 * jax.random.normal(jax.random.fold_in(_tk, 500 + 39), (1250, 32), jnp.float32)
        _rk = jax.random.fold_in(_tk, 7)
        W_top1 = 0.0354441 * jax.random.normal(jax.random.fold_in(_tk, 801), (796, 512), jnp.float32)
        W_top2 = 0.0441942 * jax.random.normal(jax.random.fold_in(_tk, 802), (512, 256), jnp.float32)
        W_top3 = 0.0625 * jax.random.normal(jax.random.fold_in(_tk, 803), (256, 1), jnp.float32)
        b_top1 = jnp.zeros((512,), jnp.float32)
        b_top2 = jnp.zeros((256,), jnp.float32)
        return (dense_ctx, ids, tbl_0, tbl_1, tbl_2, tbl_3, tbl_4, tbl_5, tbl_6, tbl_7, tbl_8, tbl_9, tbl_10, tbl_11, tbl_12, tbl_13, tbl_14, tbl_15, tbl_16, tbl_17, tbl_18, tbl_19, tbl_20, tbl_21, tbl_22, tbl_23, tbl_24, tbl_25, tbl_26, tbl_27, tbl_28, tbl_29, tbl_30, tbl_31, tbl_32, tbl_33, tbl_34, tbl_35, tbl_36, tbl_37, tbl_38, tbl_39, W_top1, b_top1, W_top2, b_top2, W_top3)
    dense_ctx, ids, tbl_0, tbl_1, tbl_2, tbl_3, tbl_4, tbl_5, tbl_6, tbl_7, tbl_8, tbl_9, tbl_10, tbl_11, tbl_12, tbl_13, tbl_14, tbl_15, tbl_16, tbl_17, tbl_18, tbl_19, tbl_20, tbl_21, tbl_22, tbl_23, tbl_24, tbl_25, tbl_26, tbl_27, tbl_28, tbl_29, tbl_30, tbl_31, tbl_32, tbl_33, tbl_34, tbl_35, tbl_36, tbl_37, tbl_38, tbl_39, W_top1, b_top1, W_top2, b_top2, W_top3 = _rec_inputs()

    def _L0_rec_setup():
        import jax, jax.numpy as jnp
        import numpy as np
        NUM_FIELDS = 40
        _I_IDX, _J_IDX = np.triu_indices(NUM_FIELDS, k=1)
        key = jax.random.key(seed)
        k1, k2 = jax.random.split(key)
        batch, num_fields, embed_dim = (1024, NUM_FIELDS, 32)
        num_interactions = num_fields * (num_fields - 1) // 2
        embeddings = jax.random.normal(k1, (batch, num_fields, embed_dim), dtype=jnp.float32)
        W = jax.random.normal(k2, (num_interactions, embed_dim, embed_dim), dtype=jnp.float32)
        return {'embeddings': embeddings, 'W': W}
    _L0_rec_all = _L0_rec_setup()
    _L0_rec_in = {k: v for k, v in _L0_rec_all.items() if k in ('W',)}
    del _L0_rec_all
    return {'dense_ctx': dense_ctx, 'ids': ids, 'tbl_0': tbl_0, 'tbl_1': tbl_1, 'tbl_2': tbl_2, 'tbl_3': tbl_3, 'tbl_4': tbl_4, 'tbl_5': tbl_5, 'tbl_6': tbl_6, 'tbl_7': tbl_7, 'tbl_8': tbl_8, 'tbl_9': tbl_9, 'tbl_10': tbl_10, 'tbl_11': tbl_11, 'tbl_12': tbl_12, 'tbl_13': tbl_13, 'tbl_14': tbl_14, 'tbl_15': tbl_15, 'tbl_16': tbl_16, 'tbl_17': tbl_17, 'tbl_18': tbl_18, 'tbl_19': tbl_19, 'tbl_20': tbl_20, 'tbl_21': tbl_21, 'tbl_22': tbl_22, 'tbl_23': tbl_23, 'tbl_24': tbl_24, 'tbl_25': tbl_25, 'tbl_26': tbl_26, 'tbl_27': tbl_27, 'tbl_28': tbl_28, 'tbl_29': tbl_29, 'tbl_30': tbl_30, 'tbl_31': tbl_31, 'tbl_32': tbl_32, 'tbl_33': tbl_33, 'tbl_34': tbl_34, 'tbl_35': tbl_35, 'tbl_36': tbl_36, 'tbl_37': tbl_37, 'tbl_38': tbl_38, 'tbl_39': tbl_39, 'W_top1': W_top1, 'b_top1': b_top1, 'W_top2': W_top2, 'b_top2': b_top2, 'W_top3': W_top3, 'L0_rec_W': _L0_rec_in['W']}

def reference(dense_ctx, ids, tbl_0, tbl_1, tbl_2, tbl_3, tbl_4, tbl_5, tbl_6, tbl_7, tbl_8, tbl_9, tbl_10, tbl_11, tbl_12, tbl_13, tbl_14, tbl_15, tbl_16, tbl_17, tbl_18, tbl_19, tbl_20, tbl_21, tbl_22, tbl_23, tbl_24, tbl_25, tbl_26, tbl_27, tbl_28, tbl_29, tbl_30, tbl_31, tbl_32, tbl_33, tbl_34, tbl_35, tbl_36, tbl_37, tbl_38, tbl_39, W_top1, b_top1, W_top2, b_top2, W_top3, L0_rec_W):
    import jax
    import jax.numpy as jnp

    def _L0_rec_ref(embeddings, W):
        import jax, jax.numpy as jnp
        import numpy as np
        NUM_FIELDS = 40
        _I_IDX, _J_IDX = np.triu_indices(NUM_FIELDS, k=1)
        vi = embeddings[:, _I_IDX, :]
        vj = embeddings[:, _J_IDX, :]
        return jnp.einsum('bke,kef,bkf->bk', vi, W, vj)
    e = jnp.stack([tbl_0[ids[:, 0]], tbl_1[ids[:, 1]], tbl_2[ids[:, 2]], tbl_3[ids[:, 3]], tbl_4[ids[:, 4]], tbl_5[ids[:, 5]], tbl_6[ids[:, 6]], tbl_7[ids[:, 7]], tbl_8[ids[:, 8]], tbl_9[ids[:, 9]], tbl_10[ids[:, 10]], tbl_11[ids[:, 11]], tbl_12[ids[:, 12]], tbl_13[ids[:, 13]], tbl_14[ids[:, 14]], tbl_15[ids[:, 15]], tbl_16[ids[:, 16]], tbl_17[ids[:, 17]], tbl_18[ids[:, 18]], tbl_19[ids[:, 19]], tbl_20[ids[:, 20]], tbl_21[ids[:, 21]], tbl_22[ids[:, 22]], tbl_23[ids[:, 23]], tbl_24[ids[:, 24]], tbl_25[ids[:, 25]], tbl_26[ids[:, 26]], tbl_27[ids[:, 27]], tbl_28[ids[:, 28]], tbl_29[ids[:, 29]], tbl_30[ids[:, 30]], tbl_31[ids[:, 31]], tbl_32[ids[:, 32]], tbl_33[ids[:, 33]], tbl_34[ids[:, 34]], tbl_35[ids[:, 35]], tbl_36[ids[:, 36]], tbl_37[ids[:, 37]], tbl_38[ids[:, 38]], tbl_39[ids[:, 39]]], axis=1)
    z = _L0_rec_ref(e, L0_rec_W)
    z = z.reshape(z.shape[0], -1)
    h = jnp.concatenate([z, dense_ctx], axis=1)
    h = jnp.maximum(h @ W_top1 + b_top1, 0.0)
    h = jnp.maximum(h @ W_top2 + b_top2, 0.0)
    y = h @ W_top3
    return y

_drawn_inputs = setup_inputs


def setup_inputs(seed=0):
    import zlib

    import numpy as np

    out = dict(_drawn_inputs(seed))
    spreads = {'b_top1': (0.0, 0.1), 'b_top2': (0.0, 0.1)}
    factors = {}
    for name, (base, spread) in spreads.items():
        noise = np.random.default_rng([zlib.crc32(name.encode()), seed]).standard_normal(out[name].shape)
        drawn = base * np.exp(spread * noise) if base else spread * noise
        out[name] = jnp.asarray(drawn.astype(out[name].dtype))
    for name, factor in factors.items():
        out[name] = (out[name] * factor).astype(out[name].dtype)
    return out
```

```python
from contextlib import ExitStack

import numpy as np

import concourse.bass as bass
from concourse import mybir

F32 = mybir.dt.float32
F32R = mybir.dt.float32r
I32 = mybir.dt.int32
ACT = mybir.ActivationFunctionType
ALU = mybir.AluOpType

PART = 128
BATCH, FIELDS, EMB, DENSE = 2048, 40, 32, 16
HID1, HID2 = 512, 256
CHUNK = 512
CHUNKS = BATCH // CHUNK
BT = CHUNK // PART
Q = PART // EMB
GROUPS = FIELDS // Q
SLOTS = 5
HALVES = CHUNKS * GROUPS // SLOTS
PAIRS = FIELDS * (FIELDS - 1) // 2
WCOLS = PAIRS * EMB
STAGE = 1920
STAGES = WCOLS // STAGE
QUADS = GROUPS * (GROUPS + 1) // 2
PER_KT = PART // (Q * Q)
KT = -(-QUADS // PER_KT)
DENSE_ROW = Q * (PER_KT - 1)
M1, M2 = HID1 // PART, HID2 // PART

USES_PER_GROUP = Q + 1
USE_H1 = GROUPS * USES_PER_GROUP
USE_H2 = USE_H1 + M1
USE_Y = USE_H2 + M2
USES = USE_Y + 1
BIAS_KEEP = 2


DRAINED0, Z_DRAINED0, REDUCED0, MULTIPLIED0, Y0 = 1, 1, 1, 2, 16


def weight_col(i, j):
    return (i * (i - 1) // 2 + j) * EMB


def quads_of(g):
    first = g * (g + 1) // 2
    at = max(g + 1 - BIAS_KEEP, 0)
    for c in range(g + 1):
        yield first + c, c, c == at and g + 1 < GROUPS


def tiles_of(g, c):
    for r in reversed(range(Q)):
        v = Q if c < g else r
        if v:
            yield r, v


def tile_span(kt, r):
    there = []
    for g in range(GROUPS):
        for n, c, _ in quads_of(g):
            if n // PER_KT == kt and r in [x for x, _ in tiles_of(g, c)]:
                there.append(n)
    return there[0], there[-1]


def build(nc, ids, tables, dense, wt, w1, b1, w2, b2, w3, out):
    ctx = ExitStack()
    with ctx:
        def sb(name, shape, dt=F32):
            return ctx.enter_context(nc.sbuf_tensor(name, shape, dt))

        def sem(name):
            return ctx.enter_context(nc.semaphore(name))

        weights = sb("weights", [PART, WCOLS + EMB], F32R)
        rows = sb("rows", [PART, SLOTS, BT, Q, EMB])
        split = sb("split", [PART, BT * Q, 2, 2, EMB], F32R)
        stacks = sb("stacks", [PART, 2 * Q, CHUNK], F32R)
        eT = sb("eT", [PART, GROUPS, CHUNK])
        prods = sb("prods", [PART, 2, Q, CHUNK])
        zs = sb("zs", [PART, KT, CHUNK])
        w1s = sb("w1s", [PART, KT, HID1])
        w2s = sb("w2s", [PART, M1, HID2])
        w3s = sb("w3s", [PART, M2])
        b1s = sb("b1s", [PART, M1])
        b2s = sb("b2s", [PART, M2])
        idx = sb("idx", [PART, SLOTS, BT * Q], I32)
        ident = sb("ident", [PART, PART], F32R)
        place = sb("place", [PART, PART + 3 * EMB], F32R)
        select = sb("select", [PART, EMB + DENSE_ROW])
        stage = prods[:, :, :, :].rearrange("p a r n -> p a (r n)")
        ident_raw = eT[:, 0, 0:PART]
        h1s = eT[:, 0:M1, :]
        h2s = zs[:, 0:M2, :]
        y_row = zs[0:1, M2, :]

        tps = ctx.enter_context(nc.psum_tensor("tps", [PART, Q, CHUNK], F32))
        zps = ctx.enter_context(nc.psum_tensor("zps", [PART, 2, CHUNK], F32))
        scratch = ctx.enter_context(nc.psum_tensor("scratch", [PART, 2, CHUNK], F32))

        def twice(s):
            r = rows[:, s].rearrange("p b f e -> p (b f) e").unsqueeze(2)
            return r.to_broadcast([PART, BT * Q, 2, EMB])

        ids_loaded = [sem(f"ids_loaded{s}") for s in range(SLOTS)]
        rows_gathered = [sem(f"rows_gathered{s}") for s in range(SLOTS)]
        w_loaded = [sem(f"w_loaded{s}") for s in range(2)]
        slot_open = sem("slot_open")
        w_hi = sem("w_hi")
        w_lo = sem("w_lo")
        ident_built = sem("ident_built")
        consts_built = sem("consts_built")
        mlp_loaded = sem("mlp_loaded")
        dense_loaded = sem("dense_loaded")
        hi_split = sem("hi_split")
        lo_split = sem("lo_split")
        scratch_filled = sem("scratch_filled")
        scratch_drained = sem("scratch_drained")
        t_filled = sem("t_filled")
        multiplied = sem("multiplied")
        reduced = sem("reduced")
        z_drained = sem("z_drained")
        y_stored = sem("y_stored")

        block = ctx.enter_context(nc.Block())

        @block.sync
        def _(sp):
            for s in range(SLOTS):
                sp.dma_start(idx[:, s, :], ids[0, s]).then_inc(ids_loaded[s], 16)
            for k in range(STAGES):
                if k >= 2:
                    sp.wait_ge(w_lo, k - 1)
                for quad in range(Q):
                    sp.dma_start(stage[quad * EMB:(quad + 1) * EMB, k % 2, 0:STAGE],
                                 wt[:, k * STAGE:(k + 1) * STAGE]).then_inc(w_loaded[k % 2], 16)
            with sp.Fori(1, HALVES) as h:
                for s in range(SLOTS):
                    sp.wait_ge(rows_gathered[s], h * (16 * BT * Q))
                    sp.dma_start(idx[:, s, :], ids[h, s]).then_inc(ids_loaded[s], 16)

        @block.gpsimd
        def _(pool):
            pool.memset(ident_raw, 0.0).then_inc(ident_built, 1)
            pool.wait_ge(ident_built, 1)
            pool.affine_select(out=ident_raw, in_=ident_raw, compare_op=ALU.not_equal, fill=1.0, base=0,
                               pattern=[[-1, PART]], channel_multiplier=1).then_inc(ident_built, 1)

            def gather(s, field0):
                for f in range(Q):
                    for b in range(BT):
                        k = b * Q + f
                        pool.indirect_dma_start(
                            rows[:, s, b, f, :], None, tables[field0 + f],
                            bass.IndirectOffsetOnAxis(ap=idx[:, s, k:k + 1], axis=0),
                        ).then_inc(rows_gathered[s], 16)

            for s in range(SLOTS):
                pool.wait_ge(ids_loaded[s], 16)
                gather(s, s * Q)
            for s in range(SLOTS):
                pool.wait_ge(ids_loaded[s], 32)
                pool.wait_ge(lo_split, s + 1)
                gather(s, (SLOTS + s) * Q)
            with pool.Fori(1, CHUNKS) as t:
                for g in range(GROUPS):
                    s = g % SLOTS
                    pool.wait_ge(ids_loaded[s], t * 32 + 16 * (g // SLOTS + 1))
                    pool.wait_ge(lo_split, t * GROUPS + (g - SLOTS + 1))
                    pool.sem_inc(slot_open, 1)
                    gather(s, g * Q)

        @block.scalar
        def _(act):
            for k in range(STAGES):
                act.wait_ge(w_loaded[k % 2], 16 * Q * (k // 2 + 1))
                act.activation(weights[:, k * STAGE:(k + 1) * STAGE], stage[:, k % 2, 0:STAGE],
                               ACT.Copy).then_inc(w_hi, 1)
            for dst, src in ((w1s, w1), (w2s, w2), (b1s, b1), (b2s, b2)):
                act.dma_start(dst[:], src).then_inc(mlp_loaded, 16)
            act.dma_start(w3s[:], w3).then_inc(y_stored, Y0)
            act.sem_inc(scratch_drained, DRAINED0)
            act.sem_inc(z_drained, Z_DRAINED0)

            with act.Fori(0, CHUNKS) as t:
                act.wait_ge(y_stored, Y0 + t * 16)
                for r in range(Q):
                    act.dma_start(zs[EMB * r + DENSE_ROW:EMB * (r + 1), KT - 1, :],
                                  dense[r * Q:(r + 1) * Q, bass.ts(t, CHUNK)]).then_inc(dense_loaded, 16)

                def drain(use, dst, func=ACT.Copy, bias=0.0):
                    act.wait_ge(scratch_filled, t * USES + (use + 1))
                    width = dst.shape[0]
                    act.activation(dst, scratch[0:width, use % 2, :], func, bias=bias).then_inc(scratch_drained, 1)

                def split_hi(g):
                    s = g % SLOTS
                    act.wait_ge(rows_gathered[s], t * (32 * BT * Q) + 16 * BT * Q * (g // SLOTS + 1))
                    if g:
                        act.wait_ge(scratch_filled, t * USES + g * USES_PER_GROUP - 1)
                    act.activation(split[:, :, :, 0, :], twice(s), ACT.Copy).then_inc(hi_split, 1)

                def drain_group(g):
                    split_hi(g)
                    for f in range(Q):
                        drain(g * USES_PER_GROUP + f, stacks[:, (g % 2) * Q + f, :])
                    drain(g * USES_PER_GROUP + Q, eT[:, g, :])

                def drain_z(kt):
                    act.wait_ge(reduced, REDUCED0 + t * QUADS + min((kt + 1) * PER_KT, QUADS))
                    if kt < KT - 1:
                        act.activation(zs[:, kt, :], zps[:, kt % 2, :], ACT.Copy).then_inc(z_drained, 1)
                    else:
                        for r in range(Q):
                            part = slice(EMB * r, EMB * r + DENSE_ROW)
                            last = act.activation(zs[part, kt, :], zps[part, kt % 2, :], ACT.Copy)
                        last.then_inc(z_drained, 1)

                drain_group(0)
                for g in range(GROUPS):
                    for n, c, stacks_next in quads_of(g):
                        if stacks_next:
                            drain_group(g + 1)
                        if n and n % PER_KT == 0:
                            drain_z(n // PER_KT - 1)
                drain_z(KT - 1)
                act.wait_ge(mlp_loaded, 16 * 4)
                for m in range(M1):
                    drain(USE_H1 + m, h1s[:, m, :], ACT.Relu, b1s[:, m:m + 1])
                for m in range(M2):
                    drain(USE_H2 + m, h2s[:, m, :], ACT.Relu, b2s[:, m:m + 1])
                drain(USE_Y, y_row)
                act.wait_ge(scratch_drained, DRAINED0 + t * USES + USES)
                act.dma_start(out[0:1, bass.ts(t, CHUNK)], y_row).then_inc(y_stored, 16)
            act.wait_ge(y_stored, Y0 + 16 * CHUNKS)

        @block.vector
        def _(dve):
            dve.memset(place[:, :].bitcast(F32), 0.0).then_inc(consts_built, 1)
            dve.memset(select[:, :], 0.0).then_inc(consts_built, 1)
            dve.memset(weights[:, WCOLS:].bitcast(F32), 0.0).then_inc(consts_built, 1)
            dve.wait_ge(consts_built, 3)
            for r in range(Q):
                dve.memset(select[EMB * r:EMB * (r + 1), DENSE_ROW + r:DENSE_ROW + r + 1], 1.0).then_inc(consts_built, 1)
            dve.wait_ge(ident_built, 2)
            dve.tensor_copy(ident[:, :], ident_raw).then_inc(consts_built, 1)
            for r in range(2):
                part = slice(EMB * r, EMB * (r + 1))
                dve.tensor_copy(place[part, 3 * EMB:4 * EMB], ident_raw[part, part]).then_inc(consts_built, 1)
            low = slice(PART // 2, PART)
            for k in range(STAGES):
                dve.wait_ge(w_hi, k + 1)
                part = weights[low, k * STAGE:(k + 1) * STAGE]
                dve.tensor_tensor(part, stage[low, k % 2, 0:STAGE], part.bitcast(F32),
                                  ALU.subtract).then_inc(w_lo, 1)
            dve.wait_ge(w_lo, STAGES)

            dve.sem_inc(multiplied, MULTIPLIED0)

            with dve.Fori(0, CHUNKS) as t:
                def split_lo(g):
                    dve.wait_ge(hi_split, t * GROUPS + (g + 1))
                    dve.tensor_tensor(split[:, :, :, 1, :], twice(g % SLOTS), split[:, :, :, 0, :].bitcast(F32),
                                      ALU.subtract).then_inc(lo_split, 1)

                split_lo(0)
                for g in range(GROUPS):
                    for n, c, stacks_next in quads_of(g):
                        if stacks_next:
                            split_lo(g + 1)
                        if c == 0:
                            dve.wait_ge(scratch_drained, DRAINED0 + t * USES + (g + 1) * USES_PER_GROUP)
                        dve.wait_ge(reduced, REDUCED0 + t * QUADS + max(n - 1, 0))
                        for pair in range(2):
                            dve.wait_ge(t_filled, t * (2 * QUADS) + (2 * n + pair + 1))
                            r0, nr, np_ = 2 * pair, 2, PART
                            if c == g:
                                r0, nr, np_ = (1, 1, EMB) if pair == 0 else (2, 2, 3 * EMB)
                            dve.tensor_tensor(prods[0:np_, n % 2, r0:r0 + nr, :], tps[0:np_, r0:r0 + nr, :],
                                              eT[0:np_, c:c + 1, :].to_broadcast([np_, nr, CHUNK]),
                                              ALU.mult).then_inc(multiplied, 1)

        @block.tensor
        def _(pe):
            pe.wait_ge(consts_built, 10)
            pe.wait_ge(w_lo, STAGES)
            pe.sem_inc(reduced, REDUCED0)

            with pe.Fori(0, CHUNKS) as t:
                def claim(use):
                    pe.wait_ge(scratch_drained, DRAINED0 + t * USES + max(use - 1, 0))

                def stack_group(g):
                    pe.wait_ge(lo_split, t * GROUPS + (g + 1))
                    for f in range(Q):
                        use = g * USES_PER_GROUP + f
                        claim(use)
                        for b in range(BT):
                            field = split[:, b * Q + f].rearrange("p d a e -> p (d a e)")
                            last = pe.matmul(scratch[:, use % 2, b * PART:(b + 1) * PART],
                                             field, ident[:, :],
                                             start=True, stop=True)
                        last.then_inc(scratch_filled, 1)
                    use = g * USES_PER_GROUP + Q
                    claim(use)
                    for f in range(Q):
                        if f == Q - 1:
                            pe.wait_ge(scratch_drained, DRAINED0 + t * USES + use)
                        last = pe.matmul(scratch[:, use % 2, :], place[:, (3 - f) * EMB:(3 - f) * EMB + PART],
                                         stacks[:, (g % 2) * Q + f, :], start=f == 0, stop=f == Q - 1)
                    last.then_inc(scratch_filled, 1)

                def transform(g, n, c):
                    there = [r for r, _ in tiles_of(g, c)]
                    for pair in range(2):
                        pe.wait_ge(multiplied, MULTIPLIED0 + t * (2 * QUADS) + (2 * n - 1 + pair))
                        for r in (2 * pair, 2 * pair + 1):
                            if r in there:
                                at = weight_col(g * Q + r, c * Q)
                                last = pe.matmul(tps[:, r, :], weights[:, at:at + PART],
                                                 stacks[:, (g % 2) * Q + r, :], start=True, stop=True)
                        last.then_inc(t_filled, 1)

                def reduce(g, n, c):
                    kt, slot = n // PER_KT, n % PER_KT
                    if slot == 0:
                        pe.wait_ge(z_drained, Z_DRAINED0 + t * KT + max(kt - 1, 0))
                    pe.wait_ge(multiplied, MULTIPLIED0 + t * (2 * QUADS) + (2 * n + 2))
                    for r, v in tiles_of(g, c):
                        first, final = tile_span(kt, r)
                        at = DENSE_ROW - Q * slot
                        last = pe.matmul(zps[EMB * r:EMB * (r + 1), kt % 2, :],
                                         select[0:EMB * v, at:at + EMB], prods[0:EMB * v, n % 2, r, :],
                                         start=n == first, stop=n == final)
                    last.then_inc(reduced, 1)

                before = None
                stack_group(0)
                for g in range(GROUPS):
                    for n, c, stacks_next in quads_of(g):
                        if stacks_next:
                            stack_group(g + 1)
                        transform(g, n, c)
                        if before is not None:
                            reduce(*before)
                        before = (g, n, c)
                reduce(*before)

                pe.wait_ge(mlp_loaded, 16 * 4)
                pe.wait_ge(y_stored, Y0)
                pe.wait_ge(dense_loaded, t * (16 * Q) + 16 * Q)
                pe.wait_ge(z_drained, Z_DRAINED0 + t * KT + KT)
                for m in range(M1):
                    claim(USE_H1 + m)
                    for k in range(KT):
                        last = pe.matmul(scratch[:, (USE_H1 + m) % 2, :], w1s[:, k, m * PART:(m + 1) * PART],
                                         zs[:, k, :], start=k == 0, stop=k == KT - 1)
                    last.then_inc(scratch_filled, 1)
                for m in range(M2):
                    claim(USE_H2 + m)
                    for k in range(M1):
                        if m == 0:
                            pe.wait_ge(scratch_drained, DRAINED0 + t * USES + (USE_H1 + k + 1))
                        last = pe.matmul(scratch[:, (USE_H2 + m) % 2, :], w2s[:, k, m * PART:(m + 1) * PART],
                                         h1s[:, k, :], start=k == 0, stop=k == M1 - 1)
                    last.then_inc(scratch_filled, 1)
                pe.wait_ge(scratch_drained, DRAINED0 + t * USES + (USE_H2 + M2))
                for k in range(M2):
                    last = pe.matmul(scratch[0:1, USE_Y % 2, :], w3s[:, k:k + 1], h2s[:, k, :],
                                     start=k == 0, stop=k == M2 - 1)
                last.then_inc(scratch_filled, 1)


def kernel(**inputs):
    import concourse.bacc as bacc
    from concourse.bass_utils import run_bass_kernel_spmd

    x = {name: np.asarray(a) for name, a in inputs.items()}

    ids = x["ids"].reshape(CHUNKS, BT, PART, GROUPS, Q).transpose(0, 3, 2, 1, 4)
    ids = ids.reshape(HALVES, SLOTS, PART, BT * Q)

    number = {}
    for a in range(FIELDS):
        for b in range(a + 1, FIELDS):
            number[a, b] = len(number)
    order = [number[j, i] for i in range(FIELDS) for j in range(i)]
    wt = x["L0_rec_W"][order].transpose(2, 0, 1).reshape(EMB, WCOLS)

    w1 = np.zeros((KT, PART, HID1), x["W_top1"].dtype)
    for g in range(GROUPS):
        for n, c, _ in quads_of(g):
            for r, v in tiles_of(g, c):
                for q in range(v):
                    row = number[c * Q + q, g * Q + r]
                    w1[n // PER_KT, EMB * r + Q * (n % PER_KT) + q] = x["W_top1"][row]
    for d in range(DENSE):
        w1[KT - 1, EMB * (d // Q) + DENSE_ROW + d % Q] = x["W_top1"][PAIRS + d]

    arrays = {
        "ids": ids,
        "dense": x["dense_ctx"].T,
        "wt": wt,
        "w1": w1.transpose(1, 0, 2),
        "b1": x["b_top1"].reshape(M1, PART).T,
        "w2": x["W_top2"].reshape(M1, PART, HID2).transpose(1, 0, 2),
        "b2": x["b_top2"].reshape(M2, PART).T,
        "w3": x["W_top3"].reshape(M2, PART).T,
    }
    for f in range(FIELDS):
        arrays[f"tbl_{f}"] = x[f"tbl_{f}"]
    arrays = {f"in_{name}": np.ascontiguousarray(a) for name, a in arrays.items()}

    nc = bacc.Bacc("TRN2", target_bir_lowering=False, num_devices=1)
    aps = {name: nc.dram_tensor(name, a.shape, mybir.dt.from_np(a.dtype), kind="ExternalInput").ap()
           for name, a in arrays.items()}
    out = nc.dram_tensor("out_y", (BATCH, 1), F32, kind="ExternalOutput").ap()
    build(nc, aps["in_ids"], [aps[f"in_tbl_{f}"] for f in range(FIELDS)], aps["in_dense"], aps["in_wt"],
          aps["in_w1"], aps["in_b1"], aps["in_w2"], aps["in_b2"], aps["in_w3"], out.rearrange("b o -> o b"))
    r = run_bass_kernel_spmd(nc, [arrays], core_ids=[0])
    return r.results[0]["out_y"]
```

```python
from contextlib import ExitStack

import numpy as np

import concourse.bass as bass
from concourse import mybir

F32 = mybir.dt.float32
F32R = mybir.dt.float32r
I32 = mybir.dt.int32
ACT = mybir.ActivationFunctionType
ALU = mybir.AluOpType

PART = 128
BATCH, FIELDS, EMB, DENSE = 2048, 40, 32, 16
HID1, HID2 = 512, 256
CHUNK = 512
CHUNKS = BATCH // CHUNK
Q = PART // EMB
GROUPS = FIELDS // Q
GATHERS = CHUNK // EMB
SLOTS = 5
PAIRS = FIELDS * (FIELDS - 1) // 2
WCOLS = PAIRS * EMB
STAGE = 1920
STAGES = WCOLS // STAGE
QUADS = GROUPS * (GROUPS + 1) // 2
PER_KT = PART // (Q * Q)
KT = -(-QUADS // PER_KT)
DENSE_ROW = Q * (PER_KT - 1)
M1, M2 = HID1 // PART, HID2 // PART

USES = GROUPS * Q + M1 + M2 + 1

TRANSPOSE, SPLIT, STACK = "transpose", "split", "stack"
STEPS = [(TRANSPOSE, 0, Q + 2), (SPLIT, 0, Q + 1)] + [(STACK, f, Q - f) for f in range(Q)]

CONSTS = 3 + 3 * Q

Z_DRAINED0, REDUCED0, MULTIPLIED0, Y0 = 1, 1, 2, 16


def weight_col(i, j):
    return (i * (i - 1) // 2 + j) * EMB


def quads_of(g):
    for c in range(g + 1):
        steps = [(what, f) for what, f, ahead in STEPS if c == max(g + 1 - ahead, 0)]
        yield g * (g + 1) // 2 + c, c, steps


def tiles_of(g, c):
    for r in reversed(range(Q)):
        v = Q if c < g else r
        if v:
            yield r, v


def tile_span(kt, r):
    there = []
    for g in range(GROUPS):
        for n, c, _ in quads_of(g):
            if n // PER_KT == kt and r in [x for x, _ in tiles_of(g, c)]:
                there.append(n)
    return there[0], there[-1]


def first_use(g):
    return (g - 1) * Q


def mlp_use(last):
    return (GROUPS - last) * Q


def build(nc, ids, bases, table, dense, wt, w1, b1, w2, b2, w3, out):
    ctx = ExitStack()
    with ctx:
        def sb(name, shape, dt=F32):
            return ctx.enter_context(nc.sbuf_tensor(name, shape, dt))

        def sem(name):
            return ctx.enter_context(nc.semaphore(name))

        weights = sb("weights", [PART, WCOLS + EMB], F32R)
        rows = sb("rows", [PART, SLOTS, CHUNK])
        eT = sb("eT", [PART, GROUPS, CHUNK])
        hi = sb("hi", [PART, CHUNK], F32R)
        lo = sb("lo", [PART, CHUNK], F32R)
        stacks = sb("stacks", [PART, 2 * Q, CHUNK], F32R)
        prods = sb("prods", [PART, 2, Q, CHUNK])
        zs = sb("zs", [PART, KT, CHUNK])
        h1s = sb("h1s", [PART, M1 - 1, CHUNK])
        w1s = sb("w1s", [PART, KT, HID1])
        w2s = sb("w2s", [PART, M1, HID2])
        w3s = sb("w3s", [PART, M2])
        b1s = sb("b1s", [PART, M1])
        b2s = sb("b2s", [PART, M2])
        idx_all = sb("idx_all", [PART, GROUPS, CHUNKS, GATHERS], I32)
        idx = sb("idx", [PART, GROUPS, GATHERS], I32)
        base = sb("base", [PART, GROUPS], I32)
        place = sb("place", [PART, Q, PART + EMB], F32R)
        select = sb("select", [PART, EMB + DENSE_ROW])
        stage = prods[:, :, :, :].rearrange("p a r n -> p a (r n)")
        ident = zs[:, 0, 0:PART]
        h1_parts = [h1s[:, m, :] for m in range(M1 - 1)] + [zs[:, M2 + 1, :]]
        h2s = zs[:, 0:M2, :]
        y_row = zs[0:1, M2, :]

        tps = ctx.enter_context(nc.psum_tensor("tps", [PART, Q, CHUNK], F32))
        zps = ctx.enter_context(nc.psum_tensor("zps", [PART, 2, CHUNK], F32))
        scratch = ctx.enter_context(nc.psum_tensor("scratch", [PART, 2, CHUNK], F32))

        ids_loaded = sem("ids_loaded")
        ids_based = sem("ids_based")
        idx_copied = [sem(f"idx_copied{g}") for g in range(GROUPS)]
        rows_gathered = [sem(f"rows_gathered{s}") for s in range(SLOTS)]
        slot_open = sem("slot_open")
        w_loaded = [sem(f"w_loaded{s}") for s in range(2)]
        w_hi = sem("w_hi")
        w_lo = sem("w_lo")
        ident_built = sem("ident_built")
        consts_built = sem("consts_built")
        mlp_loaded = sem("mlp_loaded")
        dense_loaded = sem("dense_loaded")
        transposed = sem("transposed")
        hi_split = sem("hi_split")
        lo_split = sem("lo_split")
        scratch_filled = sem("scratch_filled")
        scratch_drained = sem("scratch_drained")
        t_filled = sem("t_filled")
        multiplied = sem("multiplied")
        reduced = sem("reduced")
        z_drained = sem("z_drained")
        y_stored = sem("y_stored")

        def uses(t, use):
            return t * USES + (Q + use + 1)

        block = ctx.enter_context(nc.Block())

        @block.sync
        def _(sp):
            sp.dma_start(idx_all[:], ids).then_inc(ids_loaded, 16)
            sp.dma_start(base[:], bases).then_inc(ids_loaded, 16)
            for k in range(STAGES):
                if k >= 2:
                    sp.wait_ge(w_lo, k - 1)
                for quad in range(Q):
                    sp.dma_start(stage[quad * EMB:(quad + 1) * EMB, k % 2, 0:STAGE],
                                 wt[:, k * STAGE:(k + 1) * STAGE]).then_inc(w_loaded[k % 2], 16)
            sp.wait_ge(ids_based, GROUPS)
            with sp.Fori(1, CHUNKS) as t:
                for g in range(GROUPS):
                    sp.wait_ge(rows_gathered[g % SLOTS], (t * (GROUPS // SLOTS) + (g // SLOTS - 1)) * (16 * GATHERS))
                    sp.dma_start(idx[:, g, :], idx_all[:, g, bass.ds(t, 1), :]).then_inc(idx_copied[g], 16)

        @block.gpsimd
        def _(pool):
            pool.memset(ident, 0.0).then_inc(ident_built, 1)
            pool.wait_ge(ident_built, 1)
            pool.affine_select(out=ident, in_=ident, compare_op=ALU.not_equal, fill=1.0, base=0,
                               pattern=[[-1, PART]], channel_multiplier=1).then_inc(ident_built, 1)

            def gather(g, row_ids):
                for m in range(GATHERS):
                    pool.indirect_dma_start(
                        rows[:, g % SLOTS, m * EMB:(m + 1) * EMB], None, table,
                        bass.IndirectOffsetOnAxis(ap=row_ids[:, m:m + 1], axis=0),
                    ).then_inc(rows_gathered[g % SLOTS], 16)

            for g in range(GROUPS):
                pool.wait_ge(ids_based, g + 1)
                if g >= SLOTS:
                    pool.wait_ge(transposed, g - SLOTS + 1)
                gather(g, idx_all[:, g, 0, :])
            with pool.Fori(1, CHUNKS) as t:
                for g in range(GROUPS):
                    pool.wait_ge(idx_copied[g], t * 16)
                    pool.wait_ge(transposed, t * GROUPS + (g - SLOTS + 1))
                    pool.sem_inc(slot_open, 1)
                    gather(g, idx[:, g, :])

        @block.scalar
        def _(act):
            for k in range(STAGES):
                act.wait_ge(w_loaded[k % 2], 16 * Q * (k // 2 + 1))
                act.activation(weights[:, k * STAGE:(k + 1) * STAGE], stage[:, k % 2, 0:STAGE],
                               ACT.Copy).then_inc(w_hi, 1)
            for dst, src in ((w1s, w1), (w2s, w2), (b1s, b1), (b2s, b2)):
                act.dma_start(dst[:], src).then_inc(mlp_loaded, 16)
            act.dma_start(w3s[:], w3).then_inc(y_stored, Y0)
            act.sem_inc(z_drained, Z_DRAINED0)
            act.wait_ge(consts_built, CONSTS)

            def drain(count, use, dst, func=ACT.Copy, bias=0.0):
                act.wait_ge(scratch_filled, count)
                act.activation(dst, scratch[0:dst.shape[0], use % 2, :], func, bias=bias).then_inc(scratch_drained, 1)

            def split_hi(t, g, stacked):
                act.wait_ge(transposed, t * GROUPS + (g + 1))
                if stacked is not None:
                    act.wait_ge(scratch_filled, stacked)
                act.activation(hi[:, :], eT[:, g % GROUPS, :], ACT.Copy).then_inc(hi_split, 1)

            def drain_z(t, kt):
                act.wait_ge(reduced, REDUCED0 + t * QUADS + min((kt + 1) * PER_KT, QUADS))
                if kt < KT - 1:
                    act.activation(zs[:, kt, :], zps[:, kt % 2, :], ACT.Copy).then_inc(z_drained, 1)
                else:
                    for r in range(Q):
                        part = slice(EMB * r, EMB * r + DENSE_ROW)
                        last = act.activation(zs[part, kt, :], zps[part, kt % 2, :], ACT.Copy)
                    last.then_inc(z_drained, 1)

            def chunk(t, last):
                act.wait_ge(y_stored, Y0 + t * 16)
                for r in range(Q):
                    act.dma_start(zs[EMB * r + DENSE_ROW:EMB * (r + 1), KT - 1, :],
                                  dense[r * Q:(r + 1) * Q, bass.ts(t, CHUNK)]).then_inc(dense_loaded, 16)
                for g in range(GROUPS):
                    for n, c, steps in quads_of(g):
                        for what, f in steps if not (last and g == GROUPS - 1) else ():
                            use = first_use(g + 1) + f
                            if what == SPLIT:
                                split_hi(t, g + 1, uses(t, use - 1) if g else uses(t, -1))
                            if what == STACK:
                                drain(uses(t, use), use, stacks[:, (g + 1) % 2 * Q + f, :])
                        if n and n % PER_KT == 0:
                            drain_z(t, n // PER_KT - 1)
                drain_z(t, KT - 1)
                act.wait_ge(mlp_loaded, 16 * 4)
                use = mlp_use(last)
                for m in range(M1):
                    drain(uses(t, use + m), use + m, h1_parts[m], ACT.Relu, b1s[:, m:m + 1])
                use += M1
                for m in range(M2):
                    drain(uses(t, use + m), use + m, h2s[:, m, :], ACT.Relu, b2s[:, m:m + 1])
                use += M2
                drain(uses(t, use), use, y_row)
                act.wait_ge(scratch_drained, uses(t, use))
                act.dma_start(out[0:1, bass.ts(t, CHUNK)], y_row).then_inc(y_stored, 16)

            split_hi(0, 0, None)
            for f in range(Q):
                drain(f + 1, f, stacks[:, f, :])
            with act.Fori(0, CHUNKS - 1) as t:
                chunk(t, False)
            chunk(CHUNKS - 1, True)
            act.wait_ge(y_stored, Y0 + 16 * CHUNKS)

        @block.vector
        def _(dve):
            dve.wait_ge(ids_loaded, 32)
            for g in range(GROUPS):
                group = idx_all[:, g].rearrange("p t m -> p (t m)")
                dve.tensor_tensor(group, group, base[:, g:g + 1].to_broadcast([PART, CHUNKS * GATHERS]),
                                  ALU.add).then_inc(ids_based, 1)
            dve.memset(place[:, :, :].bitcast(F32), 0.0).then_inc(consts_built, 1)
            dve.memset(select[:, :], 0.0).then_inc(consts_built, 1)
            dve.memset(weights[:, WCOLS:].bitcast(F32), 0.0).then_inc(consts_built, 1)
            dve.wait_ge(consts_built, 3)
            dve.wait_ge(ident_built, 2)
            for r in range(Q):
                part = slice(EMB * r, EMB * (r + 1))
                dve.memset(select[part, DENSE_ROW + r:DENSE_ROW + r + 1], 1.0).then_inc(consts_built, 1)
                for to in (EMB, 3 * EMB):
                    dve.tensor_copy(place[part, r, to:to + EMB], ident[part, part]).then_inc(consts_built, 1)
            low = slice(PART // 2, PART)
            for k in range(STAGES):
                dve.wait_ge(w_hi, k + 1)
                part = weights[low, k * STAGE:(k + 1) * STAGE]
                dve.tensor_tensor(part, stage[low, k % 2, 0:STAGE], part.bitcast(F32),
                                  ALU.subtract).then_inc(w_lo, 1)
            dve.wait_ge(w_lo, STAGES)
            dve.sem_inc(multiplied, MULTIPLIED0)

            def transpose(t, g):
                slot = g % GROUPS % SLOTS
                dve.wait_ge(rows_gathered[slot], (t * (GROUPS // SLOTS) + (g // SLOTS + 1)) * (16 * GATHERS))
                dve.transpose(eT[:, g % GROUPS, :], rows[:, slot, :]).then_inc(transposed, 1)

            def split_lo(t, g):
                dve.wait_ge(hi_split, t * GROUPS + (g + 1))
                dve.tensor_tensor(lo[:, :], eT[:, g % GROUPS, :], hi[:, :].bitcast(F32),
                                  ALU.subtract).then_inc(lo_split, 1)

            def chunk(t, last):
                for g in range(GROUPS):
                    for n, c, steps in quads_of(g):
                        for what, _ in steps if not (last and g == GROUPS - 1) else ():
                            if what == TRANSPOSE:
                                dve.wait_ge(multiplied, MULTIPLIED0 + t * (2 * QUADS) + 2 * n)
                                transpose(t, g + 1)
                            if what == SPLIT:
                                split_lo(t, g + 1)
                        if c == 0:
                            dve.wait_ge(transposed, t * GROUPS + (g + 1))
                        dve.wait_ge(reduced, REDUCED0 + t * QUADS + max(n - 1, 0))
                        for pair in range(2):
                            dve.wait_ge(t_filled, t * (2 * QUADS) + (2 * n + pair + 1))
                            r0, nr, width = 2 * pair, 2, PART
                            if c == g:
                                r0, nr, width = (1, 1, EMB) if pair == 0 else (2, 2, 3 * EMB)
                            dve.tensor_tensor(prods[0:width, n % 2, r0:r0 + nr, :], tps[0:width, r0:r0 + nr, :],
                                              eT[0:width, c:c + 1, :].to_broadcast([width, nr, CHUNK]),
                                              ALU.mult).then_inc(multiplied, 1)

            transpose(0, 0)
            split_lo(0, 0)
            with dve.Fori(0, CHUNKS - 1) as t:
                chunk(t, False)
            chunk(CHUNKS - 1, True)

        @block.tensor
        def _(pe):
            pe.wait_ge(consts_built, CONSTS)
            pe.wait_ge(w_lo, STAGES)
            pe.sem_inc(reduced, REDUCED0)

            def stack(use, g, f):
                for part, at in ((hi, EMB), (lo, 0)):
                    last = pe.matmul(scratch[:, use % 2, :], place[:, f, at:at + PART], part[:, :],
                                     start=at > 0, stop=at == 0)
                last.then_inc(scratch_filled, 1)

            def chunk(t, last_chunk):
                def claim(use):
                    pe.wait_ge(scratch_drained, uses(t, use - 2 + (use == 0)))

                def transform(g, n, c):
                    if c == 0:
                        pe.wait_ge(scratch_drained, uses(t, first_use(g) + Q - 1))
                    there = [r for r, _ in tiles_of(g, c)]
                    for pair in range(2):
                        pe.wait_ge(multiplied, MULTIPLIED0 + t * (2 * QUADS) + (2 * n - 1 + pair))
                        for r in (2 * pair, 2 * pair + 1):
                            if r in there:
                                at = weight_col(g * Q + r, c * Q)
                                last = pe.matmul(tps[:, r, :], weights[:, at:at + PART],
                                                 stacks[:, (g % 2) * Q + r, :], start=True, stop=True)
                        last.then_inc(t_filled, 1)

                def reduce(g, n, c):
                    kt, slot = n // PER_KT, n % PER_KT
                    if slot == 0:
                        pe.wait_ge(z_drained, Z_DRAINED0 + t * KT + max(kt - 1, 0))
                    pe.wait_ge(multiplied, MULTIPLIED0 + t * (2 * QUADS) + (2 * n + 2))
                    for r, v in tiles_of(g, c):
                        first, final = tile_span(kt, r)
                        at = DENSE_ROW - Q * slot
                        last = pe.matmul(zps[EMB * r:EMB * (r + 1), kt % 2, :],
                                         select[0:EMB * v, at:at + EMB], prods[0:EMB * v, n % 2, r, :],
                                         start=n == first, stop=n == final)
                    last.then_inc(reduced, 1)

                before = None
                for g in range(GROUPS):
                    for n, c, steps in quads_of(g):
                        transform(g, n, c)
                        for what, f in steps if not (last_chunk and g == GROUPS - 1) else ():
                            if what == STACK:
                                use = first_use(g + 1) + f
                                claim(use)
                                pe.wait_ge(lo_split, t * GROUPS + (g + 2))
                                stack(use, g + 1, f)
                        if before is not None:
                            reduce(*before)
                        before = (g, n, c)
                reduce(*before)

                pe.wait_ge(mlp_loaded, 16 * 4)
                pe.wait_ge(y_stored, Y0)
                pe.wait_ge(dense_loaded, t * (16 * Q) + 16 * Q)
                pe.wait_ge(z_drained, Z_DRAINED0 + t * KT + KT)
                use = mlp_use(last_chunk)
                for m in range(M1):
                    claim(use + m)
                    for k in range(KT):
                        last = pe.matmul(scratch[:, (use + m) % 2, :], w1s[:, k, m * PART:(m + 1) * PART],
                                         zs[:, k, :], start=k == 0, stop=k == KT - 1)
                    last.then_inc(scratch_filled, 1)
                for m in range(M2):
                    claim(use + M1 + m)
                    for k in range(M1):
                        if m == 0:
                            pe.wait_ge(scratch_drained, uses(t, use + k))
                        last = pe.matmul(scratch[:, (use + M1 + m) % 2, :], w2s[:, k, m * PART:(m + 1) * PART],
                                         h1_parts[k], start=k == 0, stop=k == M1 - 1)
                    last.then_inc(scratch_filled, 1)
                pe.wait_ge(scratch_drained, uses(t, use + M1 + M2 - 1))
                for k in range(M2):
                    last = pe.matmul(scratch[0:1, (use + M1 + M2) % 2, :], w3s[:, k:k + 1], h2s[:, k, :],
                                     start=k == 0, stop=k == M2 - 1)
                last.then_inc(scratch_filled, 1)

            pe.wait_ge(lo_split, 1)
            for f in range(Q):
                if f >= 2:
                    pe.wait_ge(scratch_drained, f - 1)
                stack(f, 0, f)
            with pe.Fori(0, CHUNKS - 1) as t:
                chunk(t, False)
            chunk(CHUNKS - 1, True)


def kernel(**inputs):
    import concourse.bacc as bacc
    from concourse.bass_utils import run_bass_kernel_spmd

    x = {name: np.asarray(a) for name, a in inputs.items()}

    ids = x["ids"].reshape(CHUNKS, GATHERS, EMB, GROUPS, Q).transpose(4, 2, 3, 0, 1)
    ids = ids.reshape(PART, GROUPS, CHUNKS, GATHERS)
    tables = [x[f"tbl_{f}"] for f in range(FIELDS)]
    first = np.cumsum([0] + [len(a) for a in tables[:-1]], dtype=np.int32)
    bases = np.repeat(first.reshape(GROUPS, Q).T, EMB, axis=0)

    number = {}
    for a in range(FIELDS):
        for b in range(a + 1, FIELDS):
            number[a, b] = len(number)
    order = [number[j, i] for i in range(FIELDS) for j in range(i)]
    wt = x["L0_rec_W"][order].transpose(2, 0, 1).reshape(EMB, WCOLS)

    w1 = np.zeros((KT, PART, HID1), x["W_top1"].dtype)
    for g in range(GROUPS):
        for n, c, _ in quads_of(g):
            for r, v in tiles_of(g, c):
                for q in range(v):
                    row = number[c * Q + q, g * Q + r]
                    w1[n // PER_KT, EMB * r + Q * (n % PER_KT) + q] = x["W_top1"][row]
    for d in range(DENSE):
        w1[KT - 1, EMB * (d // Q) + DENSE_ROW + d % Q] = x["W_top1"][PAIRS + d]

    arrays = {
        "ids": ids,
        "bases": bases,
        "table": np.concatenate(tables),
        "dense": x["dense_ctx"].T,
        "wt": wt,
        "w1": w1.transpose(1, 0, 2),
        "b1": x["b_top1"].reshape(M1, PART).T,
        "w2": x["W_top2"].reshape(M1, PART, HID2).transpose(1, 0, 2),
        "b2": x["b_top2"].reshape(M2, PART).T,
        "w3": x["W_top3"].reshape(M2, PART).T,
    }
    arrays = {f"in_{name}": np.ascontiguousarray(a) for name, a in arrays.items()}

    nc = bacc.Bacc("TRN2", target_bir_lowering=False, num_devices=1)
    aps = {name: nc.dram_tensor(name, a.shape, mybir.dt.from_np(a.dtype), kind="ExternalInput").ap()
           for name, a in arrays.items()}
    out = nc.dram_tensor("out_y", (BATCH, 1), F32, kind="ExternalOutput").ap()
    build(nc, aps["in_ids"], aps["in_bases"], aps["in_table"], aps["in_dense"], aps["in_wt"],
          aps["in_w1"], aps["in_b1"], aps["in_w2"], aps["in_b2"], aps["in_w3"], out.rearrange("b o -> o b"))
    r = run_bass_kernel_spmd(nc, [arrays], core_ids=[0])
    return r.results[0]["out_y"]
```

```python
from contextlib import ExitStack

import numpy as np

import concourse.bass as bass
from concourse import mybir

F32 = mybir.dt.float32
F32R = mybir.dt.float32r
I32 = mybir.dt.int32
ACT = mybir.ActivationFunctionType
ALU = mybir.AluOpType

PART = 128
BATCH, FIELDS, EMB, DENSE = 2048, 40, 32, 16
HID1, HID2 = 512, 256
CHUNK = 256
CHUNKS = BATCH // CHUNK
Q = PART // EMB
GROUPS = FIELDS // Q
GATHERS = CHUNK // EMB
PAIRS = FIELDS * (FIELDS - 1) // 2
WCOLS = PAIRS * EMB
BLOCK = WCOLS // Q
PIECE = 480
PIECES = BLOCK // PIECE
LOADS = [(0, 2), (2, 5), (5, 8), (8, PIECES)]
RAW_PRODS = 8
W_BUFS = 3
BANK = 512
QUADS = GROUPS * (GROUPS + 1) // 2
PER_KT = PART // (Q * Q)
KT = -(-QUADS // PER_KT)
DENSE_ROW = Q * (PER_KT - 1)
M1, M2 = HID1 // PART, HID2 // PART

TRANSPOSE, SPLIT, STACK, MLP = "transpose", "split", "stack", "mlp"
REDUCE, REDUCE_BEFORE, LAST_MLP = "reduce", "reduce_before", "last_mlp"
STEPS = [(TRANSPOSE, 0, 5), (SPLIT, 0, 4)] + [(STACK, p, 3 - p) for p in range(Q // 2)]
COPY_Z_AT = PER_KT * (KT - 1) + 2
LOOK_AHEAD = 3
STACK_BUFS = [0, 1, 2, 0, 1, 0, 1, 0, 1, 2]
PROD_SLOTS = 4
SUMS_BEHIND = 2

CONSTS = 4 + 5 * Q

LAYERS = [(KT, M1), (M1, M2), (M2, 1)]
MLP_OUTS = M1 + M2 + 1
MLP_STEPS = [(layer_, m_, k_) for layer_, (ins_, outs_) in enumerate(LAYERS)
             for m_ in range(outs_) for k_ in range(ins_)]
MLP_PACE = [3, 2, 1, 1, 2, 3, 2, 2, 2, 2, 1, 2, 2, 2, 1] + [1] * 10

EARLY = {36: (0, 0, 0), 37: (0, 0, 1), 38: (0, 0, 2), 39: (0, 0, 3), 43: (0, 0, 4),
         45: (0, 1, 0), 47: (0, 1, 1), 49: (0, 1, 2), 51: (0, 1, 3), 53: (0, 0, 5)}
LATE = [(layer_, m_, k_) for layer_, (ins_, outs_) in enumerate(LAYERS)
        for k_ in range(ins_) for m_ in range(outs_) if (layer_, m_, k_) not in EARLY.values()]


def mlp_out(layer, m):
    return sum(outs for _, outs in LAYERS[:layer]) + m


def wait(engine, semaphore, count):
    if not (isinstance(count, int) and count <= 0):
        engine.wait_ge(semaphore, count)


def weight_col(i, j):
    return (i * (i - 1) // 2 + j) * EMB


def quads_of(g):
    for c in range(g + 1):
        yield g * (g + 1) // 2 + c, c


def steps_of(n, last):
    return [(what, g, p) for g in range(GROUPS + LOOK_AHEAD) for what, p, ahead in STEPS
            if g // GROUPS * QUADS + (g % GROUPS) * (g % GROUPS + 1) // 2 - ahead == n
            and not (last and g >= GROUPS)]


def tensor_steps(n, first, last):
    if n >= SUMS_BEHIND:
        yield REDUCE, n - SUMS_BEHIND
    elif not first:
        yield REDUCE_BEFORE, n - SUMS_BEHIND + QUADS
    stacks = [(what, (g, p)) for what, g, p in steps_of(n, last) if what == STACK]
    mlp = []
    if not first and n < len(MLP_PACE):
        done = sum(MLP_PACE[:n])
        mlp = [(MLP, step) for step in MLP_STEPS[done:done + MLP_PACE[n]]]
    cut = [len(mlp) * at // (len(stacks) + 1) for at in range(len(stacks) + 2)]
    for at in range(len(stacks) + 1):
        yield from mlp[cut[at]:cut[at + 1]]
        yield from stacks[at:at + 1]
    if last and n in EARLY:
        yield LAST_MLP, EARLY[n]


def tiles_of(g, c):
    for r in reversed(range(Q)):
        v = Q if c < g else r
        if v:
            yield r, v


def reuse(n, slots):
    if n >= slots:
        return n - slots + 1
    return max(last for last in range(QUADS) if last % slots == n % slots) + 1 - QUADS


def tile_span(kt, r):
    there = []
    for g in range(GROUPS):
        for n, c in quads_of(g):
            if n // PER_KT == kt and r in [x for x, _ in tiles_of(g, c)]:
                there.append(n)
    return there[0], there[-1]


def build(nc, ids, bases, table, dense, wt, w1, b1, w2, b2, w3, out):
    ctx = ExitStack()
    with ctx:
        def sb(name, shape, dt=F32):
            return ctx.enter_context(nc.sbuf_tensor(name, shape, dt))

        def sem(name):
            return ctx.enter_context(nc.semaphore(name))

        weights = sb("weights", [PART, WCOLS + EMB], F32R)
        rows = sb("rows", [PART, GROUPS, CHUNK])
        eT = sb("eT", [PART, GROUPS, CHUNK])
        hi = sb("hi", [PART, 2, CHUNK], F32R)
        lo = sb("lo", [PART, 2, CHUNK], F32R)
        stacks = sb("stacks", [PART, 3, Q, CHUNK], F32R)
        prods = sb("prods", [PART, PROD_SLOTS, Q, CHUNK])
        z_all = sb("z_all", [PART, 2 * KT - 1, CHUNK])
        z_new = z_all[:, 0:KT - 1, :]
        zs = z_all[:, KT - 1:, :]
        h1s = sb("h1s", [PART, M1, CHUNK])
        h2s = sb("h2s", [PART, M2, CHUNK])
        y_row = sb("y_row", [1, CHUNK])
        w1s = sb("w1s", [PART, KT, HID1])
        w2s = sb("w2s", [PART, M1, HID2])
        w3s = sb("w3s", [PART, M2])
        b1s = sb("b1s", [PART, M1])
        b2s = sb("b2s", [PART, M2])
        idx_all = sb("idx_all", [PART, GROUPS, CHUNKS, GATHERS], I32)
        idx = sb("idx", [PART, GROUPS, GATHERS], I32)
        base = sb("base", [PART, GROUPS], I32)
        place = sb("place", [PART, Q, PART + EMB], F32R)
        select = sb("select", [PART, EMB + DENSE_ROW])
        w_parts = sb("w_parts", [PART, 2 * W_BUFS, PIECE], F32R)
        w_hi = [w_parts[:, 2 * j, :] for j in range(W_BUFS)]
        w_lo = [w_parts[:, 2 * j + 1, :] for j in range(W_BUFS)]
        prods_flat = prods[:, :, :, :].rearrange("p a r n -> p (a r n)")
        z_flat = z_all[:, :, :].rearrange("p k n -> p (k n)")
        ident = z_flat[:, (2 * KT - 1) * CHUNK - PART:]
        raw = [prods_flat[:, j * PIECE:(j + 1) * PIECE] for j in range(RAW_PRODS)]
        raw += [z_flat[:, j * PIECE:(j + 1) * PIECE] for j in range(PIECES - RAW_PRODS)]
        w_place = stacks[:, 0, :, :].rearrange("p a n -> p (a n)")[:, 0:Q * (PART + 2 * EMB)]
        w_place = w_place.rearrange("p (q n) -> p q n", q=Q)

        tps = ctx.enter_context(nc.psum_tensor("tps", [PART, 2, Q, CHUNK], F32))
        zps = ctx.enter_context(nc.psum_tensor("zps", [PART, 2, BANK], F32))
        stack_ps = ctx.enter_context(nc.psum_tensor("stack_ps", [PART, Q // 2, CHUNK], F32))
        mlp_ps = ctx.enter_context(nc.psum_tensor("mlp_ps", [PART, BANK], F32))
        t_banks = tps[:, :, :, :].rearrange("p a r n -> p (a r n)")
        t_banks = [t_banks[:, at:at + BANK] for at in range(0, 2 * Q * CHUNK, BANK)]
        stack_bank = stack_ps[:, :, :].rearrange("p a n -> p (a n)")
        w_banks = [[bank[:, 0:PIECE] for bank in t_banks],
                   [bank[:, 0:PIECE] for bank in (zps[:, 0], zps[:, 1], stack_bank, mlp_ps)]]
        between_banks = [mlp_ps[:, 0:CHUNK]] * MLP_OUTS
        last_banks = [bank[:, 0:CHUNK] for bank in (mlp_ps, stack_bank, t_banks[2], t_banks[3],
                                                      t_banks[0], t_banks[1], zps[:, KT % 2])]

        ids_loaded = sem("ids_loaded")
        ids_based = sem("ids_based")
        idx_copied = [sem(f"idx_copied{g}") for g in range(GROUPS)]
        rows_gathered = [sem(f"rows_gathered{g}") for g in range(GROUPS)]
        slot_open = sem("slot_open")
        w_loaded = [sem(f"w_loaded{s}") for s in range(len(LOADS))]
        w_hi_split = sem("w_hi_split")
        w_lo_split = sem("w_lo_split")
        w_stacked = sem("w_stacked")
        w_act_drained = sem("w_act_drained")
        w_dve_drained = sem("w_dve_drained")
        ident_built = sem("ident_built")
        consts_built = sem("consts_built")
        mlp_loaded = sem("mlp_loaded")
        dense_loaded = sem("dense_loaded")
        transposed = sem("transposed")
        hi_split = sem("hi_split")
        lo_split = sem("lo_split")
        stack_filled = sem("stack_filled")
        stack_drained = sem("stack_drained")
        mlp_filled = sem("mlp_filled")
        mlp_drained = sem("mlp_drained")
        t_filled = sem("t_filled")
        multiplied = sem("multiplied")
        reduced = sem("reduced")
        z_drained = sem("z_drained")
        z_copied = sem("z_copied")
        y_stored = sem("y_stored")

        block = ctx.enter_context(nc.Block())

        @block.sync
        def _(sp):
            sp.dma_start(idx_all[:], ids).then_inc(ids_loaded, 16)
            sp.dma_start(base[:], bases).then_inc(ids_loaded, 16)
            for (a, b), loaded in zip(LOADS, w_loaded):
                flat, first = (prods_flat, 0) if b <= RAW_PRODS else (z_flat, RAW_PRODS)
                dst = flat[:, (a - first) * PIECE:(b - first) * PIECE].rearrange("p (j n) -> p j n", n=PIECE)
                sp.dma_start(dst, wt[:, a:b, :]).then_inc(loaded, 16)
            for dst, src in ((w1s, w1), (w2s, w2), (w3s, w3), (b1s, b1), (b2s, b2)):
                sp.dma_start(dst[:], src).then_inc(mlp_loaded, 16)
            sp.wait_ge(ids_based, GROUPS)

            def copy_ids(t):
                for g in range(GROUPS):
                    sp.wait_ge(rows_gathered[g], t * (16 * GATHERS))
                    sp.dma_start(idx[:, g, :], idx_all[:, g, bass.ds(t, 1), :]).then_inc(idx_copied[g], 16)

            def load_dense(t):
                sp.wait_ge(z_drained, t * KT + KT)
                for r in range(Q):
                    sp.dma_start(zs[EMB * r + DENSE_ROW:EMB * (r + 1), KT - 1, :],
                                 dense[r * Q:(r + 1) * Q, bass.ts(t, CHUNK)]).then_inc(dense_loaded, 16)

            copy_ids(1)
            with sp.Fori(2, CHUNKS) as t:
                load_dense(t - 2)
                copy_ids(t)
            load_dense(CHUNKS - 2)
            load_dense(CHUNKS - 1)

        @block.gpsimd
        def _(pool):
            pool.memset(ident, 0.0).then_inc(ident_built, 1)
            pool.wait_ge(ident_built, 1)
            pool.affine_select(out=ident, in_=ident, compare_op=ALU.not_equal, fill=1.0, base=0,
                               pattern=[[-1, PART]], channel_multiplier=1).then_inc(ident_built, 1)

            def gather(g, row_ids):
                for m in range(GATHERS):
                    pool.indirect_dma_start(
                        rows[:, g, m * EMB:(m + 1) * EMB], None, table,
                        bass.IndirectOffsetOnAxis(ap=row_ids[:, m:m + 1], axis=0),
                    ).then_inc(rows_gathered[g], 16)

            for g in range(GROUPS):
                pool.wait_ge(ids_based, g + 1)
                gather(g, idx_all[:, g, 0, :])
            with pool.Fori(1, CHUNKS) as t:
                for g in range(GROUPS):
                    pool.wait_ge(idx_copied[g], t * 16)
                    pool.wait_ge(transposed, t * GROUPS + (g + 1 - GROUPS))
                    pool.sem_inc(slot_open, 1)
                    gather(g, idx[:, g, :])

        @block.scalar
        def _(act):
            def split_raw(j):
                load = [a <= j < b for a, b in LOADS].index(True)
                act.wait_ge(w_loaded[load], 16)
                wait(act, w_stacked, Q * (j - W_BUFS + 1))
                act.activation(w_hi[j % W_BUFS], raw[j], ACT.Copy).then_inc(w_hi_split, 1)

            split_raw(0)
            split_raw(1)
            for j in range(PIECES):
                for r in range(Q // 2):
                    act.wait_ge(w_stacked, Q * j + r + 1)
                    at = r * BLOCK + j * PIECE
                    act.activation(weights[:, at:at + PIECE], w_banks[j % 2][r], ACT.Copy).then_inc(w_act_drained, 1)
                if j + 2 < PIECES:
                    split_raw(j + 2)

            def split_hi(t, g):
                act.wait_ge(transposed, t * GROUPS + (g + 1))
                wait(act, stack_filled, (t * GROUPS + g - 1) * (Q // 2))
                act.activation(hi[:, g % 2, :], eT[:, g % GROUPS, :], ACT.Copy).then_inc(hi_split, 1)

            def drain_stack(t, g, p):
                act.wait_ge(stack_filled, (t * GROUPS + g) * (Q // 2) + (p + 1))
                act.activation(stacks[:, STACK_BUFS[g % GROUPS], 2 * p:2 * p + 2, :], stack_ps[:, :, :], ACT.Copy).then_inc(stack_drained, 1)

            def drain_z(t, kt):
                act.wait_ge(reduced, t * QUADS + min((kt + 1) * PER_KT, QUADS))
                wait(act, z_copied, t)
                dst = z_new[:, kt, :] if kt < KT - 1 else zs[:, kt, :]
                act.activation(dst, zps[:, kt % 2, 0:CHUNK], ACT.Copy).then_inc(z_drained, 1)

            def copy_z(t):
                act.wait_ge(z_drained, t * KT + (KT - 1))
                act.activation(zs[:, 0:KT - 1, :], z_new, ACT.Copy).then_inc(z_copied, 1)

            def drain_mlp(t, banks, layer, m):
                out_tile = mlp_out(layer, m)
                act.wait_ge(mlp_filled, t * MLP_OUTS + (out_tile + 1))
                if layer < 2:
                    dst, bias = [(h1s, b1s), (h2s, b2s)][layer]
                    act.activation(dst[:, m, :], banks[out_tile], ACT.Relu, bias=bias[:, m:m + 1]).then_inc(mlp_drained, 1)
                else:
                    wait(act, y_stored, t * 16)
                    act.activation(y_row[:, :], banks[out_tile][0:1, :], ACT.Copy).then_inc(mlp_drained, 1)
                    act.wait_ge(mlp_drained, t * MLP_OUTS + MLP_OUTS)
                    act.dma_start(out[0:1, bass.ts(t, CHUNK)], y_row[:, :]).then_inc(y_stored, 16)

            def chunk(t, first=False, last=False):
                for g in range(GROUPS):
                    for n, c in quads_of(g):
                        for what, ahead, _ in steps_of(n, last):
                            if what == SPLIT:
                                split_hi(t, ahead)
                        for what, which in tensor_steps(n, first, last):
                            if what == STACK:
                                drain_stack(t, *which)
                            if what == MLP and which[2] == LAYERS[which[0]][0] - 1:
                                drain_mlp(t - 1, between_banks, which[0], which[1])
                            if what == REDUCE and (which + 1) % PER_KT == 0:
                                drain_z(t, which // PER_KT)
                            if what == REDUCE_BEFORE and which == QUADS - 1:
                                drain_z(t - 1, KT - 1)
                        if n == COPY_Z_AT and not last:
                            copy_z(t)
                if last:
                    drain_z(t, KT - 1)

            for n in range(-QUADS, 0):
                for what, ahead, _ in steps_of(n, False):
                    if what == SPLIT:
                        split_hi(0, ahead)
                for what, ahead, p in steps_of(n, False):
                    if what == STACK:
                        drain_stack(0, ahead, p)
            chunk(0, first=True)
            act.wait_ge(mlp_loaded, 16 * 5)
            with act.Fori(1, CHUNKS - 1) as t:
                chunk(t)
            chunk(CHUNKS - 1, last=True)
            for layer, (_, outs) in enumerate(LAYERS):
                for m in range(outs):
                    drain_mlp(CHUNKS - 1, last_banks, layer, m)
            act.wait_ge(y_stored, 16 * CHUNKS)

        @block.vector
        def _(dve):
            dve.wait_ge(ids_loaded, 32)
            for g in range(GROUPS):
                group = idx_all[:, g].rearrange("p t m -> p (t m)")
                dve.tensor_tensor(group, group, base[:, g:g + 1].to_broadcast([PART, CHUNKS * GATHERS]),
                                  ALU.add).then_inc(ids_based, 1)
            dve.memset(place[:, :, :].bitcast(F32), 0.0).then_inc(consts_built, 1)
            dve.memset(select[:, :], 0.0).then_inc(consts_built, 1)
            dve.memset(weights[:, WCOLS:].bitcast(F32), 0.0).then_inc(consts_built, 1)
            dve.memset(w_place.bitcast(F32), 0.0).then_inc(consts_built, 1)
            dve.wait_ge(consts_built, 4)
            dve.wait_ge(ident_built, 2)
            for r in range(Q):
                part = slice(EMB * r, EMB * (r + 1))
                dve.memset(select[part, DENSE_ROW + r:DENSE_ROW + r + 1], 1.0).then_inc(consts_built, 1)
                for to in (EMB, 3 * EMB):
                    dve.tensor_copy(place[part, r, to:to + EMB], ident[part, part]).then_inc(consts_built, 1)
                for to in (2 * EMB, 3 * EMB):
                    dve.tensor_copy(w_place[part, r, to:to + EMB], ident[part, part]).then_inc(consts_built, 1)
            def split_raw(j):
                dve.wait_ge(w_hi_split, j + 1)
                dve.tensor_tensor(w_lo[j % W_BUFS], raw[j], w_hi[j % W_BUFS].bitcast(F32), ALU.subtract).then_inc(w_lo_split, 1)

            split_raw(0)
            for j in range(PIECES):
                if j + 1 < PIECES:
                    split_raw(j + 1)
                for r in range(Q // 2, Q):
                    dve.wait_ge(w_stacked, Q * j + r + 1)
                    at = r * BLOCK + j * PIECE
                    dve.tensor_copy(weights[:, at:at + PIECE], w_banks[j % 2][r]).then_inc(w_dve_drained, 1)

            def transpose(t, g):
                dve.wait_ge(rows_gathered[g % GROUPS], (t + g // GROUPS + 1) * (16 * GATHERS))
                wait(dve, multiplied, (t + g // GROUPS - 1) * QUADS + (QUADS - GROUPS + g % GROUPS + 1))
                dve.transpose(eT[:, g % GROUPS, :], rows[:, g % GROUPS, :]).then_inc(transposed, 1)

            def split_lo(t, g):
                dve.wait_ge(hi_split, t * GROUPS + (g + 1))
                dve.tensor_tensor(lo[:, g % 2, :], eT[:, g % GROUPS, :], hi[:, g % 2, :].bitcast(F32),
                                  ALU.subtract).then_inc(lo_split, 1)

            def prepare(t, n, last):
                for what, g, _ in steps_of(n, last):
                    if what == TRANSPOSE:
                        transpose(t, g)
                    if what == SPLIT:
                        split_lo(t, g)

            def chunk(t, last=False):
                for g in range(GROUPS):
                    for n, c in quads_of(g):
                        prepare(t, n, last)
                        if c == 0:
                            dve.wait_ge(transposed, t * GROUPS + (g + 1))
                        wait(dve, reduced, t * QUADS + reuse(n, PROD_SLOTS))
                        dve.wait_ge(t_filled, t * QUADS + (n + 1))
                        r0, width = (1, (Q - 1) * EMB) if c == g else (0, PART)
                        dve.tensor_tensor(prods[0:width, n % PROD_SLOTS, r0:, :], tps[0:width, n % 2, r0:, :],
                                          eT[0:width, c:c + 1, :].to_broadcast([width, Q - r0, CHUNK]),
                                          ALU.mult).then_inc(multiplied, 1)

            dve.wait_ge(w_lo_split, PIECES)
            for n in range(-QUADS, 0):
                prepare(0, n, False)
            chunk(0)
            with dve.Fori(1, CHUNKS - 1) as t:
                chunk(t)
            chunk(CHUNKS - 1, last=True)

        @block.tensor
        def _(pe):
            pe.wait_ge(consts_built, CONSTS)
            for j in range(PIECES):
                pe.wait_ge(w_lo_split, j + 1)
                wait(pe, w_act_drained, Q // 2 * (j - 1))
                wait(pe, w_dve_drained, Q // 2 * (j - 1))
                for r in range(Q):
                    pe.matmul(w_banks[j % 2][r], w_place[:, r, 2 * EMB:2 * EMB + PART], w_hi[j % W_BUFS],
                              start=True, stop=False)
                    pe.matmul(w_banks[j % 2][r], w_place[:, r, 0:PART], w_lo[j % W_BUFS],
                              start=False, stop=True).then_inc(w_stacked, 1)
            pe.wait_ge(w_act_drained, Q // 2 * PIECES)
            pe.wait_ge(w_dve_drained, Q // 2 * PIECES)

            def stack(t, g, p):
                if p == 0:
                    pe.wait_ge(lo_split, t * GROUPS + (g + 1))
                wait(pe, stack_drained, (t * GROUPS + g) * (Q // 2) + p)
                for at in range(2):
                    f = 2 * p + at
                    pe.matmul(stack_ps[:, at, :], place[:, f, EMB:EMB + PART], hi[:, g % 2, :], start=True, stop=False)
                    last = pe.matmul(stack_ps[:, at, :], place[:, f, 0:PART], lo[:, g % 2, :], start=False, stop=True)
                last.then_inc(stack_filled, 1)

            def transform(t, g, n, c):
                if c == 0:
                    pe.wait_ge(stack_drained, (t * GROUPS + g) * (Q // 2) + Q // 2)
                wait(pe, multiplied, t * QUADS + reuse(n, 2))
                for r, _ in tiles_of(g, c):
                    at = weight_col(g * Q + r, c * Q)
                    last = pe.matmul(tps[:, n % 2, r, :], weights[:, at:at + PART],
                                     stacks[:, STACK_BUFS[g], r, :], start=True, stop=True)
                last.then_inc(t_filled, 1)

            def reduce(t, n):
                g, c = [(g, c) for g in range(GROUPS) for at, c in quads_of(g) if at == n][0]
                kt, slot = n // PER_KT, n % PER_KT
                if slot == 0:
                    wait(pe, z_drained, t * KT + (kt - 1 if kt else 0))
                pe.wait_ge(multiplied, t * QUADS + (n + 1))
                for r, v in tiles_of(g, c):
                    first, final = tile_span(kt, r)
                    at = DENSE_ROW - Q * slot
                    last = pe.matmul(zps[EMB * r:EMB * (r + 1), kt % 2, 0:CHUNK],
                                     select[0:EMB * v, at:at + EMB], prods[0:EMB * v, n % PROD_SLOTS, r, :],
                                     start=n == first, stop=n == final)
                last.then_inc(reduced, 1)

            def mlp(t, banks, layer, m, k):
                out_tile = mlp_out(layer, m)
                if banks is between_banks:
                    if layer == 0 and m == 0 and k == 0:
                        pe.wait_ge(z_copied, t + 1)
                        wait(pe, mlp_drained, t * MLP_OUTS)
                    elif layer == 1 and m == 0:
                        pe.wait_ge(mlp_drained, t * MLP_OUTS + (k + 1 if k else M1))
                    elif k == 0:
                        pe.wait_ge(mlp_drained, t * MLP_OUTS + out_tile)
                else:
                    if layer == 0 and m == 0:
                        if k == 0:
                            pe.wait_ge(mlp_drained, t * MLP_OUTS)
                        if k < KT - 1:
                            pe.wait_ge(z_drained, t * KT + (k + 1))
                    elif layer > 0 and m == 0:
                        pe.wait_ge(mlp_drained, t * MLP_OUTS + (mlp_out(layer - 1, k) + 1))
                if layer == 0 and m == 0 and k == KT - 1:
                    pe.wait_ge(dense_loaded, t * (16 * Q) + 16 * Q)
                w = [w1s, w2s][layer][:, k, m * PART:(m + 1) * PART] if layer < 2 else w3s[:, k:k + 1]
                z = z_new if banks is last_banks and k < KT - 1 else zs
                x = [z[:, k, :], h1s[:, k % M1, :], h2s[:, k % M2, :]][layer]
                dst = banks[out_tile] if layer < 2 else banks[out_tile][0:1, :]
                end = k == LAYERS[layer][0] - 1
                last = pe.matmul(dst, w, x, start=k == 0, stop=end)
                if end:
                    last.then_inc(mlp_filled, 1)

            def chunk(t, first=False, last=False):
                for g in range(GROUPS):
                    for n, c in quads_of(g):
                        transform(t, g, n, c)
                        for what, which in tensor_steps(n, first, last):
                            if what == STACK:
                                stack(t, *which)
                            if what == REDUCE:
                                reduce(t, which)
                            if what == REDUCE_BEFORE:
                                reduce(t - 1, which)
                            if what == MLP:
                                mlp(t - 1, between_banks, *which)
                            if what == LAST_MLP:
                                mlp(t, last_banks, *which)
                if last:
                    reduce(t, QUADS - 2)
                    mlp(t, last_banks, *LATE[0])
                    mlp(t, last_banks, *LATE[1])
                    reduce(t, QUADS - 1)

            for n in range(-QUADS, 0):
                for what, ahead, p in steps_of(n, False):
                    if what == STACK:
                        stack(0, ahead, p)
            chunk(0, first=True)
            pe.wait_ge(mlp_loaded, 16 * 5)
            with pe.Fori(1, CHUNKS - 1) as t:
                chunk(t)
            chunk(CHUNKS - 1, last=True)
            for step in LATE[2:]:
                mlp(CHUNKS - 1, last_banks, *step)


def kernel(**inputs):
    import concourse.bacc as bacc
    from concourse.bass_utils import run_bass_kernel_spmd

    x = {name: np.asarray(a) for name, a in inputs.items()}

    ids = x["ids"].reshape(CHUNKS, GATHERS, EMB, GROUPS, Q).transpose(4, 2, 3, 0, 1)
    ids = ids.reshape(PART, GROUPS, CHUNKS, GATHERS)
    tables = [x[f"tbl_{f}"] for f in range(FIELDS)]
    first = np.cumsum([0] + [len(a) for a in tables[:-1]], dtype=np.int32)
    bases = np.repeat(first.reshape(GROUPS, Q).T, EMB, axis=0)

    number = {}
    for a in range(FIELDS):
        for b in range(a + 1, FIELDS):
            number[a, b] = len(number)
    order = [number[j, i] for i in range(FIELDS) for j in range(i)]
    wt = x["L0_rec_W"][order].transpose(2, 0, 1).reshape(EMB, Q, BLOCK)
    wt = wt.transpose(1, 0, 2).reshape(PART, PIECES, PIECE)

    w1 = np.zeros((KT, PART, HID1), x["W_top1"].dtype)
    for g in range(GROUPS):
        for n, c in quads_of(g):
            for r, v in tiles_of(g, c):
                for q in range(v):
                    row = number[c * Q + q, g * Q + r]
                    w1[n // PER_KT, EMB * r + Q * (n % PER_KT) + q] = x["W_top1"][row]
    for d in range(DENSE):
        w1[KT - 1, EMB * (d // Q) + DENSE_ROW + d % Q] = x["W_top1"][PAIRS + d]

    arrays = {
        "ids": ids,
        "bases": bases,
        "table": np.concatenate(tables),
        "dense": x["dense_ctx"].T,
        "wt": wt,
        "w1": w1.transpose(1, 0, 2),
        "b1": x["b_top1"].reshape(M1, PART).T,
        "w2": x["W_top2"].reshape(M1, PART, HID2).transpose(1, 0, 2),
        "b2": x["b_top2"].reshape(M2, PART).T,
        "w3": x["W_top3"].reshape(M2, PART).T,
    }
    arrays = {f"in_{name}": np.ascontiguousarray(a) for name, a in arrays.items()}

    nc = bacc.Bacc("TRN2", target_bir_lowering=False, num_devices=1)
    aps = {name: nc.dram_tensor(name, a.shape, mybir.dt.from_np(a.dtype), kind="ExternalInput").ap()
           for name, a in arrays.items()}
    out = nc.dram_tensor("out_y", (BATCH, 1), F32, kind="ExternalOutput").ap()
    build(nc, aps["in_ids"], aps["in_bases"], aps["in_table"], aps["in_dense"], aps["in_wt"],
          aps["in_w1"], aps["in_b1"], aps["in_w2"], aps["in_b2"], aps["in_w3"], out.rearrange("b o -> o b"))
    r = run_bass_kernel_spmd(nc, [arrays], core_ids=[0])
    return r.results[0]["out_y"]
```
